# Optimizing a Trainium2 kernel written in Bass

```python
import numpy as np
import jax
import jax.numpy as jnp

def _softmax(x, axis=-1):
    return jax.nn.softmax(x, axis=axis)

def _gelu(x):
    return jax.nn.gelu(x, approximate=True)

def _silu(x):
    return jax.nn.silu(x)

def _sigmoid(x):
    return jax.nn.sigmoid(x)

def _layernorm(x, axis=-1, eps=1e-05):
    m = jnp.mean(x, axis=axis, keepdims=True)
    v = jnp.var(x, axis=axis, keepdims=True)
    return (x - m) / jnp.sqrt(v + eps)

def _scatter_add(tgt, idx, src, axis=0):
    return tgt.at[idx].add(src)

def _segment_sum(src, seg, n):
    return jax.ops.segment_sum(src, seg, n)
kernel_name = 'mk_gnn_preln_d2_gnn_r8_38e143'

def setup_inputs(seed: int=0):
    np.random.seed(seed)
    _w = jnp.asarray

    def _rec_inputs():
        import jax
        import jax.numpy as jnp
        _gk = jax.random.key(seed)
        x = -0.0003713 + 1 * jax.random.normal(jax.random.fold_in(_gk, 1), (6250, 256), jnp.float32)
        src = jax.random.randint(jax.random.fold_in(_gk, 2), (100000,), 0, 6250, jnp.int32)
        dst = jnp.minimum((6250 * jax.random.uniform(jax.random.fold_in(_gk, 3), (100000,)) ** 2.0).astype(jnp.int32), 49999)
        _o = jnp.argsort(dst, stable=True)
        src = src[_o]
        dst = dst[_o]
        edge_attr_64 = -9.77346e-05 + 0.999888 * jax.random.normal(jax.random.fold_in(_gk, 12), (100000, 64), jnp.float32)
        edge_type_8 = jax.random.randint(jax.random.fold_in(_gk, 14), (100000,), 0, 8, jnp.int32)
        return (x, src, dst, edge_attr_64, edge_type_8)
    x, src, dst, edge_attr_64, edge_type_8 = _rec_inputs()

    def _L0_gnn_setup():
        import jax, jax.numpy as jnp
        import numpy as np
        LN2 = 0.6931471805599453
        N_ATOMS = 6250
        N_PAIRS = 100000
        F = 256
        RBF = 64
        N_RES = 3
        key = jax.random.key(seed)
        ks = jax.random.split(key, 16)
        inp = {'atomic_embedding': jax.random.normal(ks[0], (N_ATOMS, F), dtype=jnp.float32), 'f_ij': jax.random.normal(ks[1], (N_PAIRS, RBF), dtype=jnp.float32), 'idx_i': jax.random.randint(ks[2], (N_PAIRS,), 0, N_ATOMS, dtype=jnp.int32), 'idx_j': jax.random.randint(ks[3], (N_PAIRS,), 0, N_ATOMS, dtype=jnp.int32), 'G': jax.random.normal(ks[4], (F, RBF), dtype=jnp.float32), 'Wi': jax.random.normal(ks[5], (F, F), dtype=jnp.float32) * 0.05, 'bi': jax.random.normal(ks[6], (F,), dtype=jnp.float32) * 0.05, 'Wj': jax.random.normal(ks[7], (F, F), dtype=jnp.float32) * 0.05, 'bj': jax.random.normal(ks[8], (F,), dtype=jnp.float32) * 0.05, 'res_w1': jax.random.normal(ks[9], (N_RES, F, F), dtype=jnp.float32) * 0.05, 'res_b1': jax.random.normal(ks[10], (N_RES, F), dtype=jnp.float32) * 0.05, 'res_w2': jax.random.normal(ks[11], (N_RES, F, F), dtype=jnp.float32) * 0.05, 'res_b2': jax.random.normal(ks[12], (N_RES, F), dtype=jnp.float32) * 0.05, 'Wv': jax.random.normal(ks[13], (F, F), dtype=jnp.float32) * 0.05, 'bv': jax.random.normal(ks[14], (F,), dtype=jnp.float32) * 0.05}
        return inp
    _L0_gnn_all = _L0_gnn_setup()
    _L0_gnn_in = {k: v for k, v in _L0_gnn_all.items() if k in ('G', 'Wi', 'bi', 'Wj', 'bj', 'res_w1', 'res_b1', 'res_w2', 'res_b2', 'Wv', 'bv')}
    del _L0_gnn_all

    def _L1_gnn_setup():
        import jax, jax.numpy as jnp
        import numpy as np
        N, E, D, R, L = (6250, 31250, 256, 8, 3)
        key = jax.random.key(seed)
        k = jax.random.split(key, 7)
        scale = 1.0 / np.sqrt(D)
        x = jax.random.normal(k[0], (N, D), dtype=jnp.float32)
        edge_index = jax.random.randint(k[1], (2, E), 0, N, dtype=jnp.int64)
        edge_type = jax.random.randint(k[2], (E,), 0, R, dtype=jnp.int64)
        W_rel = jax.random.normal(k[3], (L, R, D, D), dtype=jnp.float32) * scale
        W_root = jax.random.normal(k[4], (L, D, D), dtype=jnp.float32) * scale
        bias = jax.random.normal(k[5], (L, D), dtype=jnp.float32) * 0.02
        return {'x': x, 'edge_index': edge_index, 'edge_type': edge_type, 'W_rel': W_rel, 'W_root': W_root, 'bias': bias}
    _L1_gnn_all = _L1_gnn_setup()
    _L1_gnn_in = {k: v for k, v in _L1_gnn_all.items() if k in ('W_rel', 'W_root', 'bias')}
    del _L1_gnn_all
    return {'x': x, 'src': src, 'dst': dst, 'edge_attr_64': edge_attr_64, 'edge_type_8': edge_type_8, 'L0_gnn_G': _L0_gnn_in['G'], 'L0_gnn_Wi': _L0_gnn_in['Wi'], 'L0_gnn_bi': _L0_gnn_in['bi'], 'L0_gnn_Wj': _L0_gnn_in['Wj'], 'L0_gnn_bj': _L0_gnn_in['bj'], 'L0_gnn_res_w1': _L0_gnn_in['res_w1'], 'L0_gnn_res_b1': _L0_gnn_in['res_b1'], 'L0_gnn_res_w2': _L0_gnn_in['res_w2'], 'L0_gnn_res_b2': _L0_gnn_in['res_b2'], 'L0_gnn_Wv': _L0_gnn_in['Wv'], 'L0_gnn_bv': _L0_gnn_in['bv'], 'L1_gnn_W_rel': _L1_gnn_in['W_rel'], 'L1_gnn_W_root': _L1_gnn_in['W_root'], 'L1_gnn_bias': _L1_gnn_in['bias']}

def reference(x, src, dst, edge_attr_64, edge_type_8, L0_gnn_G, L0_gnn_Wi, L0_gnn_bi, L0_gnn_Wj, L0_gnn_bj, L0_gnn_res_w1, L0_gnn_res_b1, L0_gnn_res_w2, L0_gnn_res_b2, L0_gnn_Wv, L0_gnn_bv, L1_gnn_W_rel, L1_gnn_W_root, L1_gnn_bias):
    import jax
    import jax.numpy as jnp

    def _L0_gnn_ref(atomic_embedding, f_ij, idx_i, idx_j, G, Wi, bi, Wj, bj, res_w1, res_b1, res_w2, res_b2, Wv, bv):
        import jax, jax.numpy as jnp
        import numpy as np
        LN2 = 0.6931471805599453
        N_ATOMS = 6250
        N_PAIRS = 100000
        F = 256
        RBF = 64
        N_RES = 3
        sp = jax.nn.softplus
        x = sp(atomic_embedding) - LN2
        x_i_prime = sp(x @ Wi.T + bi)
        x_j_all = sp(x @ Wj.T + bj)
        x_j_prime = x_j_all[idx_j]
        f_ij_prime = f_ij @ G.T
        msg = x_j_prime * f_ij_prime
        summed = jax.ops.segment_sum(msg, idx_i, num_segments=atomic_embedding.shape[0])
        v = x_i_prime + summed
        for k in range(res_w1.shape[0]):
            h = sp(v @ res_w1[k].T + res_b1[k])
            v = v + h @ res_w2[k].T + res_b2[k]
        return sp(v) @ Wv.T + bv

    def _L1_gnn_ref(x, edge_index, edge_type, W_rel, W_root, bias):
        import jax, jax.numpy as jnp
        import numpy as np
        N, E, D, R, L = (6250, 31250, 256, 8, 3)
        src, dst = (edge_index[0], edge_index[1])
        n_layers = W_rel.shape[0]
        for l in range(n_layers):
            xr = jnp.einsum('nd,rde->rne', x, W_rel[l])
            msg = xr[edge_type, src]
            agg = jax.ops.segment_sum(msg, dst, num_segments=x.shape[0])
            x = jax.nn.relu(agg + x @ W_root[l] + bias[l])
        return x
    edge_index = jnp.stack([src, dst])
    h = jnp.maximum(_layernorm(x, axis=-1), 0.0)
    x = x + _L0_gnn_ref(h, edge_attr_64, src, dst, L0_gnn_G, L0_gnn_Wi, L0_gnn_bi, L0_gnn_Wj, L0_gnn_bj, L0_gnn_res_w1, L0_gnn_res_b1, L0_gnn_res_w2, L0_gnn_res_b2, L0_gnn_Wv, L0_gnn_bv)
    h = jnp.maximum(_layernorm(x, axis=-1), 0.0)
    x = x + _L1_gnn_ref(h, edge_index, edge_type_8, L1_gnn_W_rel, L1_gnn_W_root, L1_gnn_bias)
    return x

_drawn_inputs = setup_inputs


def setup_inputs(seed=0):
    import zlib

    import numpy as np

    out = dict(_drawn_inputs(seed))
    spreads = {}
    factors = {'L0_gnn_Wi': 8.0,
     'L0_gnn_bi': 64.0,
     'L0_gnn_bj': 4.501,
     'L0_gnn_res_b1': 64.0,
     'L0_gnn_res_b2': 34.569,
     'L0_gnn_bv': 25.159,
     'L1_gnn_bias': 8.0}
    for name, (base, spread) in spreads.items():
        noise = np.random.default_rng([zlib.crc32(name.encode()), seed]).standard_normal(out[name].shape)
        drawn = base * np.exp(spread * noise) if base else spread * noise
        out[name] = jnp.asarray(drawn.astype(out[name].dtype))
    for name, factor in factors.items():
        out[name] = (out[name] * factor).astype(out[name].dtype)
    return out
```

```python
from contextlib import ExitStack

import concourse.bass as bass
from concourse import mybir

P = 128
N, E, D, RBF, REL, LAYERS, RES = 6250, 100000, 256, 64, 8, 3, 3
NT = -(-N // P)
NPAD = NT * P
TAILROWS = N - (NT - 1) * P

COLS = E // P // 4 * 4
REST = E - COLS * P
RESTFULL, RESTPART = REST // P, REST % P
U = 8
TURNS = -(-(COLS + -(-REST // P)) // U)
CH = TURNS * U
IW = CH + U

PAIR = 2 * P
PB = 8
NPAIR = -(-((E + PAIR * NT) // PAIR) // PB) * PB
PTURNS = NPAIR // PB
SLOTC = 2 * NPAIR
MW = D + 4
PADPOS = float(1 << 24)
PADROW = float(1 << 20)

LN2 = 0.6931471805599453
EPS = 1e-5


def wait(eng, sem, value):
    if not isinstance(value, int):
        eng.wait_ge(sem, value)
        if eng.engine in (mybir.EngineType.Activation, mybir.EngineType.DVE, mybir.EngineType.Pool):
            eng.nop(nofuse=True)
    elif value > 0:
        eng.wait_ge(sem, value)


class Program:

    def __init__(self, nc, ctx, a):
        self.nc, self.ctx, self.a = nc, ctx, a
        f32, i32, u8 = mybir.dt.float32, mybir.dt.int32, mybir.dt.uint8
        self.f32, self.i32, self.u8 = f32, i32, u8

        def sb(name, shape, dt=f32):
            return ctx.enter_context(nc.sbuf_tensor(name, shape, dt))

        self.xj_table = nc.dram_tensor("xj_table", [NPAD, D], f32, kind="Internal").ap()
        self.msg_slots = nc.dram_tensor("msg_slots", [(NPAIR + NT) * PAIR, MW], f32, kind="Internal").ap()
        self.edge_slots = nc.dram_tensor("edge_slots", [P * SLOTC, 2], f32, kind="Internal").ap()
        self.xr = [nc.dram_tensor(f"xr{i}", [NPAD * REL, D], f32, kind="Internal").ap() for i in range(2)]

        self.X = sb("X", [P, NT * D])
        self.V = sb("V", [P, (NT + 1) * D])
        self.WT = sb("WT", [P, 9 * 512])
        self.GT = sb("GT", [P, D])
        self.R0 = sb("R0", [P, 2 * REL * D])
        self.rawx = sb("rawx", [P, 768])
        self.work = sb("work", [P, CH * NT // 4])
        self.idx = sb("idx", [P, 9 * IW])
        self.bias9 = sb("bias9", [P, D])
        self.bcol = sb("bcol", [P, LAYERS * 2])

        self.iota = sb("iota", [P, P])
        self.ident = sb("ident", [P, P])
        self.before = sb("before", [P, P])
        self.upto = sb("upto", [P, NT])
        self.ones = sb("ones", [P, P])
        self.lastrow = sb("lastrow", [P, NT])
        self.cap = sb("cap", [P, 1])
        self.tile1 = sb("tile1", [P, 1])
        self.epsc = sb("epsc", [P, 1])

        self.cnt = sb("cnt", [P, NT])
        self.base = sb("base", [P, NT])
        self.small = sb("small", [P, 8])
        self.smalli = sb("smalli", [P, 4], i32)

        self.bank = [ctx.enter_context(nc.psum_tensor(f"bank{i}", [P, 512], f32)) for i in range(8)]

        self.s_in = [self.sem(f"gathered{k}") for k in range(PB)]

        def row(k, n=1):
            return self.idx[:, k * IW:(k + n) * IW]

        self.src, self.dst, self.typ = row(0).bitcast(i32), row(1).bitcast(i32), row(2).bitcast(i32)
        self.scan, self.key = row(0), row(2)
        self.loc_s = row(3)
        self.pos_s, self.pos_d = row(4), row(7)
        self.edge_row = row(5, 2)
        self.eq = row(8).bitcast(u8)[:, 0:CH]
        self.iotap = row(8)[0:NT, CH // 4 + 4:CH // 4 + 4 + NPAIR]
        self.fillt = row(8).bitcast(i32)[0:1, IW - 2 * NT:IW]
        self.endeq, self.diag = self.scan[0:NT, 0:NPAIR], self.scan[0:NT, NPAIR:NPAIR + NT]
        flags = self.rawx[0:1, :].bitcast(mybir.dt.int16)
        self.flag_s, self.flag_d = flags[:, 0:NPAIR], flags[:, NPAIR:2 * NPAIR]

    def sem(self, name):
        return self.ctx.enter_context(self.nc.semaphore(name))


    def count_step(self, g, eq):
        ALU = mybir.AluOpType
        return self.nc.vector.tensor_scalar(eq, self.key[:, 0:CH], self.iota[:, bass.ds(g, 1)], 0.0,
                                            ALU.is_equal, ALU.add, accum_out=self.cnt[:, bass.ds(g, 1)])

    def scan_step(self, g, eq):
        ALU = mybir.AluOpType
        return self.nc.vector.tensor_tensor_scan(self.scan[:, 0:CH], eq, eq, self.base[:, bass.ds(g, 1)],
                                                 ALU.add, ALU.max)

    def base_tensor(self, pe, ps, pb, counted, steps, sums, fills):
        nc = self.nc
        pe.wait_ge(*counted)
        nc.tensor.matmul(ps[0:NT, 500:501], self.cnt[:, :], self.ones[:, 0:1], start=True, stop=True).then_inc(sums, 1)
        pe.wait_ge(steps, 4)
        nc.tensor.matmul(ps[0:NT, 501:502], self.upto[0:NT, :], self.small[0:NT, 0:1], start=True, stop=True).then_inc(sums, 1)
        pe.wait_ge(steps, 10)
        nc.tensor.matmul(pb[:, 0:NT], self.before[:, :], self.cnt[:, :], start=True, stop=False, skip_group_check=True)
        nc.tensor.matmul(pb[:, 0:NT], self.ones[0:NT, :], self.diag[:, :], start=False, stop=True, skip_group_check=True)
        if fills:
            nc.tensor.matmul(pb[0:1, 64:64 + NT], self.small[0:NT, 2:3], self.ident[0:NT, 0:NT], start=False, stop=True,
                             skip_group_check=True)
            nc.tensor.matmul(pb[0:1, 64 + NT:64 + 2 * NT], self.small[0:NT, 1:2], self.lastrow[0:NT, :], start=False,
                             stop=True, skip_group_check=True)
        nc.tensor.matmul(ps[0:1, 0:NPAIR], self.tile1[0:NT, :], self.endeq[:, :], start=True, stop=True).then_inc(sums, 1)

    def base_vector(self, dve, ps, pb, steps, sums, flag, fills):
        nc, sm = self.nc, self.small
        ALU = mybir.AluOpType
        count = [0]

        def link(ins):
            count[0] += 1
            ins.then_inc(steps, 1)
            wait(dve, steps, count[0])

        wait(dve, sums, 1)
        link(nc.vector.tensor_scalar(self.smalli[0:NT, 0:1], ps[0:NT, 500:501], float(PAIR - 1), None, ALU.add))
        link(nc.vector.tensor_scalar(self.smalli[0:NT, 1:2], self.smalli[0:NT, 0:1], PAIR.bit_length() - 1, None,
                                     ALU.logical_shift_right))
        link(nc.vector.tensor_copy(sm[0:NT, 3:4], self.smalli[0:NT, 1:2]))
        link(nc.vector.tensor_scalar(sm[0:NT, 0:1], sm[0:NT, 3:4], 1.0, None, ALU.max))
        wait(dve, sums, 2)
        link(nc.vector.tensor_copy(sm[0:NT, 1:2], ps[0:NT, 501:502]))
        link(nc.vector.tensor_scalar(sm[0:NT, 2:3], sm[0:NT, 1:2], -1.0, None, ALU.add))
        link(nc.vector.tensor_scalar(sm[0:NT, 4:5], sm[0:NT, 1:2], sm[0:NT, 0:1], float(PAIR), ALU.subtract, ALU.mult))
        link(nc.vector.tensor_scalar(self.diag[:, :], self.ident[0:NT, 0:NT], sm[0:NT, 4:5], None, ALU.mult))
        link(nc.vector.tensor_scalar(sm[0:NT, 5:6], sm[0:NT, 2:3], self.cap[0:NT, :], None, ALU.max))
        link(nc.vector.tensor_scalar(self.endeq[:, :], self.iotap[:, :], sm[0:NT, 5:6], None, ALU.is_equal))
        wait(dve, sums, 3)
        link(nc.vector.tensor_copy(self.base[:, :], pb[:, 0:NT]))
        link(nc.vector.tensor_copy(flag[:, :], ps[0:1, 0:NPAIR]))
        if fills:
            link(nc.vector.tensor_copy(self.fillt[0:1, 0:NT], pb[0:1, 64:64 + NT]))
            link(nc.vector.tensor_tensor(self.fillt[0:1, NT:2 * NT], pb[0:1, 64 + NT:64 + 2 * NT], self.iotap[0:1, 0:NT], ALU.add))

    def join_stats(self, dve, stats, mean, var, tmp, sem, base):
        nc, ALU = self.nc, mybir.AluOpType
        s6 = stats.rearrange("p (t c) -> p t c", c=6)
        nc.vector.tensor_tensor(tmp, s6[:, :, 1], s6[:, :, 4], ALU.subtract).then_inc(sem, 1)
        nc.vector.tensor_tensor(mean, s6[:, :, 1], s6[:, :, 4], ALU.add).then_inc(sem, 1)
        wait(dve, sem, base + 2)
        nc.vector.scalar_tensor_tensor(tmp, tmp, D / 4.0, tmp, ALU.mult, ALU.mult).then_inc(sem, 1)
        nc.vector.tensor_scalar(mean, mean, 0.5, None, ALU.mult).then_inc(sem, 1)
        nc.vector.tensor_tensor(var, s6[:, :, 2], s6[:, :, 5], ALU.add).then_inc(sem, 1)
        wait(dve, sem, base + 5)
        nc.vector.tensor_tensor(var, var, tmp, ALU.add).then_inc(sem, 1)
        wait(dve, sem, base + 6)
        nc.vector.tensor_scalar(var, var, 1.0 / D, None, ALU.mult).then_inc(sem, 1)
        wait(dve, sem, base + 7)


    def prepare(self):
        nc, a, f32, i32 = self.nc, self.a, self.f32, self.i32
        ALU, ACT = mybir.AluOpType, mybir.ActivationFunctionType
        ds, bank = bass.ds, self.bank
        X, V, WT, R0, bias9 = self.X, self.V, self.WT, self.R0, self.bias9
        mask = self.work[:, :].bitcast(self.u8)
        sem = self.sem
        s_pad, s_c, s_fills = sem("p_pad"), sem("p_consts"), sem("p_fillbufs")
        s_x, s_ix, s_w, s_b = sem("p_x"), sem("p_indices"), sem("p_weights"), sem("p_biases")
        s_wt, s_wc = sem("p_transposed"), sem("p_wt_copied")
        s_ip, s_st, s_agg, s_ln, s_exp, s_nw = (sem("p_index_prep"), sem("p_stats"), sem("p_aggr"), sem("p_lnvar"),
                                                sem("p_rstd0"), sem("p_newton"))
        s_cnt, s_steps, s_sums, s_scan, s_pick, s_pos, s_fin = (
            sem("p_counted"), sem("p_base_steps"), sem("p_base_sums"), sem("p_scanned"), sem("p_picked"), sem("p_added"),
            sem("p_pos"))
        s_h, s_e, s_l = sem("p_h"), sem("p_exp"), sem("p_log")
        s_xs, s_tr, s_xst, s_mm, s_out = (sem("p_xs"), sem("p_xs_transposed"), sem("p_xst"), sem("p_projected"),
                                          sem("p_outputs"))
        s_ab, s_e2, s_l2 = sem("p_abs"), sem("p_exp2"), sem("p_log2")
        s_xjo = sem("p_xj_rows")
        s_wr = [sem(f"p_xj_written{i}") for i in range(2)]
        s_mf, s_lf = sem("p_msg_filled"), sem("p_edges_filled")

        at = [0]

        def part(n):
            at[0] += n
            return R0[:, at[0] - n:at[0]]

        hb, eb, xsb, xst, lb, xjo = ([part(n) for _ in range(2)] for n in (D, D, D, D, 2 * D, D))
        tmp = self.pos_s.bitcast(i32)
        fillm, fille = self.idx[:, 7 * IW:7 * IW + 2 * MW], self.idx[:, 7 * IW + 2 * MW:7 * IW + 2 * MW + 220]
        mean, var, rstd, nmr, t0, t1 = (part(NT) for _ in range(6))
        stats = self.scan[:, 0:6 * NT]
        squares = ([("L0_gnn_Wi", None), ("L0_gnn_Wj", None)] + [("L0_gnn_res_w1", k) for k in range(RES)]
                   + [("L0_gnn_res_w2", k) for k in range(RES)] + [("L0_gnn_Wv", None)])
        raw = [R0[:, m * 512:(m + 1) * 512] for m in range(8)] + [self.rawx[:, 0:512]]

        with nc.Block() as block:

            @block.gpsimd
            def _(eng):
                nc.gpsimd.memset(self.src[:, COLS:IW], 1 << 20).then_inc(s_pad, 1)
                nc.gpsimd.memset(self.dst[:, COLS:IW], 1 << 20).then_inc(s_pad, 1)
                nc.gpsimd.memset(self.typ[:, COLS:IW], 0).then_inc(s_pad, 1)
                nc.gpsimd.memset(X[:, (NT - 1) * D:NT * D], 0.0).then_inc(s_pad, 1)
                nc.gpsimd.memset(bias9[:, :], 0.0).then_inc(s_pad, 1)
                nc.gpsimd.memset(fillm, -1.0).then_inc(s_fills, 1)
                f2 = fille.rearrange("p (c two) -> p c two", two=2)
                nc.gpsimd.memset(f2[:, :, 0], PADROW).then_inc(s_fills, 1)
                nc.gpsimd.memset(f2[:, :, 1], -1.0).then_inc(s_fills, 1)
                nc.gpsimd.memset(self.ident[:, :], 0.0).then_inc(s_c, 1)
                nc.gpsimd.memset(self.before[:, :], 0.0).then_inc(s_c, 1)
                nc.gpsimd.memset(self.upto[:, :], 0.0).then_inc(s_c, 1)
                nc.gpsimd.memset(self.lastrow[:, :], 0.0).then_inc(s_c, 1)
                nc.gpsimd.memset(self.cap[:, :], 0.0).then_inc(s_c, 1)
                nc.gpsimd.memset(self.ones[:, :], 1.0).then_inc(s_c, 1)
                nc.gpsimd.memset(self.epsc[:, :], EPS).then_inc(s_c, 1)
                nc.gpsimd.memset(V[:, NT * D:(NT + 1) * D], 0.0).then_inc(s_c, 1)
                nc.gpsimd.iota(self.iota[:, :], pattern=[[1, P]], base=0, channel_multiplier=0,
                               allow_small_or_imprecise_dtypes=True).then_inc(s_c, 1)
                nc.gpsimd.iota(self.iotap[:, :], pattern=[[1, NPAIR]], base=0, channel_multiplier=0,
                               allow_small_or_imprecise_dtypes=True).then_inc(s_c, 1)
                nc.gpsimd.iota(self.tile1[:, :], pattern=[[0, 1]], base=1, channel_multiplier=1,
                               allow_small_or_imprecise_dtypes=True).then_inc(s_c, 1)
                wait(eng, s_c, 11)
                for m, op, fill, base, step, chan, n in (
                        (self.ident, ALU.not_equal, 1.0, 0, -1, 1, P), (self.before, ALU.is_ge, 1.0, 0, -1, 1, P),
                        (self.upto, ALU.is_gt, 1.0, 0, -1, 1, NT), (self.lastrow, ALU.is_gt, 1.0, NT - 1, 0, -1, NT),
                        (self.cap, ALU.is_gt, float(NPAIR - 1), NT - 1, 0, -1, 1)):
                    nc.gpsimd.affine_select(out=m[:, :], in_=m[:, :], compare_op=op, fill=fill, base=base,
                                            pattern=[[step, n]], channel_multiplier=chan).then_inc(s_c, 1)

                def write(t, p):
                    wait(eng, s_xjo, t + 1)
                    eng.dma_start(self.xj_table[ds(t * P, P), :], xjo[p]).then_inc(s_wr[p], 16)

                with eng.Fori(0, NT // 2) as i:
                    write(2 * i, 0)
                    write(2 * i + 1, 1)
                write(NT - 1, 0)
                wait(eng, s_wr[0], 16 * (NT - NT // 2))
                wait(eng, s_wr[1], 16 * (NT // 2))

            @block.sync
            def _(sp):
                def edges(name):
                    return a[name][0:COLS * P].rearrange("(p c) -> p c", c=COLS)

                sp.wait_ge(s_pad, 5)
                for name, to in (("src", self.src), ("dst", self.dst), ("edge_type_8", self.typ)):
                    sp.dma_start(to[:, 0:COLS], edges(name)).then_inc(s_ix, 16)
                    for c in range(RESTFULL + 1):
                        n = P if c < RESTFULL else RESTPART
                        first = COLS * P + c * P
                        sp.dma_start(to[0:n, COLS + c:COLS + c + 1],
                                     a[name][first:first + n].rearrange("(p c) -> p c", c=1)).then_inc(s_ix, 16)
                sp.dma_start(X[:, 0:(NT - 1) * D].rearrange("p (t d) -> p t d", d=D),
                             a["x"][0:(NT - 1) * P, :].rearrange("(t p) d -> p t d", p=P)).then_inc(s_x, 16)
                sp.dma_start(X[0:TAILROWS, (NT - 1) * D:NT * D], a["x"][(NT - 1) * P:N, :]).then_inc(s_x, 16)
                sp.wait_ge(s_fills, 3)
                es = self.edge_slots.rearrange("(p c) two -> p (c two)", p=P)
                for k in range(2 * SLOTC // 220):
                    sp.dma_start(es[:, k * 220:(k + 1) * 220], fille).then_inc(s_lf, 16)
                sp.wait_ge(s_steps, 14)
                with sp.Fori(0, 2 * NT) as k:
                    q = sp.value_load(self.fillt[0:1, ds(k, 1)], min_val=0, max_val=NPAIR + NT - 1)
                    sp.dma_start(self.msg_slots[ds(q * PAIR, PAIR), :].rearrange("(p j) c -> p (j c)", j=2),
                                 fillm).then_inc(s_mf, 16)
                sp.wait_ge(s_lf, 16 * (2 * SLOTC // 220))
                sp.wait_ge(s_mf, 16 * 2 * NT)

            @block.scalar
            def _(act):
                for m, (name, k) in enumerate(squares):
                    w = a[name] if k is None else a[name][k, :, :]
                    act.dma_start(raw[m].rearrange("p (h k) -> p h k", h=2), w.rearrange("(h p) k -> p h k", p=P)).then_inc(s_w, 16)
                g4 = self.rawx[:, 512:768].rearrange("p (h c r) -> p h c r", h=2, c=2)
                for c in range(2):
                    act.dma_start(g4[:, :, c, :], a["L0_gnn_G"].rearrange("(h p) r -> p h r", p=P)).then_inc(s_w, 16)
                wait(act, s_pad, 5)
                rows = [("L0_gnn_bi", 0), ("L0_gnn_bj", 1), ("L0_gnn_bv", 8)]
                for name, b in rows:
                    act.dma_start(bias9[b:b + 1, :], a[name].rearrange("(o d) -> o d", o=1)).then_inc(s_b, 16)
                act.dma_start(bias9[2:5, :], a["L0_gnn_res_b1"]).then_inc(s_b, 16)
                act.dma_start(bias9[5:8, :], a["L0_gnn_res_b2"]).then_inc(s_b, 16)
                for l in range(LAYERS):
                    for h in range(2):
                        act.dma_start(self.bcol[:, 2 * l + h:2 * l + h + 1],
                                      a["L1_gnn_bias"][l, h * P:(h + 1) * P].rearrange("(p o) -> p o", o=1)).then_inc(s_b, 16)
                nc.scalar.preload_act_table_set("natural_log_exp_and_others")
                for m in range(9):
                    wait(act, s_wt, m + 1)
                    nc.scalar.activation(WT[:, m * 512:(m + 1) * 512], bank[m % 4][:, :], ACT.Copy).then_inc(s_wc, 1)
                wait(act, s_wt, 10)
                nc.scalar.activation(self.GT[:, :], bank[4][:, 0:D], ACT.Copy).then_inc(s_wc, 1)
                wait(act, s_agg, 7)
                wait(act, s_c, 16)
                nc.scalar.activation(t0, var, ACT.Ln, bias=self.epsc[:, 0:1]).then_inc(s_ln, 1)
                wait(act, s_ln, 1)
                nc.scalar.activation(rstd, t0, ACT.Exp, scale=-0.5).then_inc(s_exp, 1)
                wait(act, s_nw, 5)
                wait(act, s_wc, 10)

                def front(t, p):
                    wait(act, s_xs, t - 1)
                    nc.scalar.activation(hb[p], X[:, ds(t * D, D)], ACT.Relu, bias=nmr[:, ds(t, 1)],
                                         scale=rstd[:, ds(t, 1)]).then_inc(s_h, 1)
                    wait(act, s_h, t + 1)
                    nc.scalar.activation(eb[p], hb[p], ACT.Exp, scale=-1.0).then_inc(s_e, 1)
                    wait(act, s_e, t + 1)
                    nc.scalar.activation(eb[p], eb[p], ACT.Ln, bias=1.0).then_inc(s_l, 1)

                def back(t, p):
                    wait(act, s_mm, t + 1)
                    wait(act, s_out, t - 1)
                    nc.scalar.activation(lb[p], bank[2 + p][:, :], ACT.Abs).then_inc(s_ab, 1)
                    wait(act, s_ab, t + 1)
                    nc.scalar.activation(lb[p], lb[p], ACT.Exp, scale=-1.0).then_inc(s_e2, 1)
                    wait(act, s_e2, t + 1)
                    nc.scalar.activation(lb[p], lb[p], ACT.Ln, bias=1.0).then_inc(s_l2, 1)

                self.skewed(act, front, back)

            @block.tensor
            def _(pe):
                pe.wait_ge(s_w, 16 * 11)
                pe.wait_ge(s_c, 16)
                for m in range(9):
                    wait(pe, s_wc, m - 3)
                    for kh in range(2):
                        for nh in range(2):
                            last = nc.tensor.transpose(bank[m % 4][:, kh * D + nh * P:kh * D + nh * P + P],
                                                       raw[m][:, nh * D + kh * P:nh * D + kh * P + P], self.ident[:, :])
                    last.then_inc(s_wt, 1)
                for nh in range(2):
                    last = nc.tensor.transpose(bank[4][:, nh * P:(nh + 1) * P], self.rawx[:, 512 + nh * P:512 + (nh + 1) * P],
                                               self.ident[:, :])
                last.then_inc(s_wt, 1)
                self.base_tensor(pe, bank[5], bank[6], (s_cnt, NT), s_steps, s_sums, True)
                pe.wait_ge(s_wc, 10)
                pe.wait_ge(s_b, 16 * 11)

                def front(t, p):
                    pe.wait_ge(s_xs, t + 1)
                    wait(pe, s_xst, t - 1)
                    for h in range(2):
                        last = nc.tensor.transpose(bank[p][:, h * P:(h + 1) * P], xsb[p][:, h * P:(h + 1) * P], self.ident[:, :])
                    last.then_inc(s_tr, 1)

                def back(t, p):
                    pe.wait_ge(s_xst, t + 1)
                    wait(pe, s_out, t - 1)
                    out = bank[2 + p]
                    for mh in range(2):
                        o = out[:, mh * P:(mh + 1) * P]
                        nc.tensor.matmul(o, bias9[:, mh * P:(mh + 1) * P], self.ident[:, 0:1].to_broadcast([P, P]),
                                         start=(mh == 0), stop=False, skip_group_check=True)
                        for k in range(2):
                            nc.tensor.matmul(o, WT[:, k * D + mh * P:k * D + mh * P + P], xst[p][:, k * P:(k + 1) * P],
                                             start=False, stop=True, skip_group_check=True)
                    o = out[:, D:2 * D]
                    nc.tensor.matmul(o, self.ident[:, 1:2].to_broadcast([P, P]), bias9[:, :], start=False, stop=False,
                                     skip_group_check=True)
                    for k in range(2):
                        last = nc.tensor.matmul(o, xst[p][:, k * P:(k + 1) * P], WT[:, 512 + k * D:512 + (k + 1) * D],
                                                start=False, stop=True, skip_group_check=True)
                    last.then_inc(s_mm, 1)

                self.skewed(pe, front, back)

            @block.vector
            def _(dve):
                wait(dve, s_ix, 16 * 3 * (RESTFULL + 2))
                rows2 = self.edge_row.rearrange("p (c two) -> p c two", two=2)
                nc.vector.scalar_tensor_tensor(rows2[:, :, 0], self.src, float(REL), self.typ, ALU.mult, ALU.add).then_inc(s_ip, 1)
                nc.vector.tensor_scalar(tmp, self.dst, P - 1, None, ALU.bitwise_and).then_inc(s_ip, 1)
                wait(dve, s_ip, 2)
                nc.vector.tensor_copy(rows2[:, :, 1], tmp).then_inc(s_ip, 1)
                wait(dve, s_ip, 3)
                nc.vector.tensor_scalar(tmp, self.src, P - 1, None, ALU.bitwise_and).then_inc(s_ip, 1)
                wait(dve, s_ip, 4)
                nc.vector.tensor_copy(self.loc_s, tmp).then_inc(s_ip, 1)
                wait(dve, s_ip, 5)
                nc.vector.tensor_scalar(tmp, self.src, P.bit_length() - 1, None, ALU.logical_shift_right).then_inc(s_ip, 1)
                wait(dve, s_ip, 6)
                nc.vector.tensor_copy(self.key, tmp).then_inc(s_ip, 1)
                wait(dve, s_ip, 7)
                nc.vector.memset(self.pos_s, 0.0).then_inc(s_ip, 1)
                wait(dve, s_ip, 8)
                wait(dve, s_c, 16)
                wait(dve, s_pad, 5)
                with dve.Fori(0, NT) as g:
                    self.count_step(g, mask[:, ds(g * CH, CH)]).then_inc(s_cnt, 1)
                wait(dve, s_x, 32)
                wait(dve, s_wc, 10)
                with dve.Fori(0, NT) as t:
                    nc.vector.bn_stats(stats[:, ds(6 * t, 6)], X[:, ds(t * D, D)]).then_inc(s_st, 1)
                wait(dve, s_st, NT)
                self.join_stats(dve, stats, mean, var, t0, s_agg, 0)
                self.base_vector(dve, bank[5], bank[6], s_steps, s_sums, self.flag_s, True)
                wait(dve, s_exp, 1)
                nc.vector.tensor_tensor(t1, rstd, rstd, ALU.mult).then_inc(s_nw, 1)
                wait(dve, s_nw, 1)
                nc.vector.scalar_tensor_tensor(t1, var, EPS, t1, ALU.add, ALU.mult).then_inc(s_nw, 1)
                wait(dve, s_nw, 2)
                nc.vector.tensor_scalar(t1, t1, -0.5, 1.5, ALU.mult, ALU.add).then_inc(s_nw, 1)
                wait(dve, s_nw, 3)
                nc.vector.tensor_tensor(rstd, rstd, t1, ALU.mult).then_inc(s_nw, 1)
                wait(dve, s_nw, 4)
                nc.vector.scalar_tensor_tensor(nmr, mean, -1.0, rstd, ALU.mult, ALU.mult).then_inc(s_nw, 1)

                def front(t, p):
                    wait(dve, s_l, t + 1)
                    wait(dve, s_tr, t - 1)
                    nc.vector.scalar_tensor_tensor(xsb[p], hb[p], -LN2, eb[p], ALU.add, ALU.add).then_inc(s_xs, 1)
                    self.scan_step(t, mask[:, ds(t * CH, CH)]).then_inc(s_scan, 1)
                    wait(dve, s_tr, t + 1)
                    wait(dve, s_mm, t - 1)
                    nc.vector.tensor_copy(xst[p], bank[p][:, 0:D]).then_inc(s_xst, 1)
                    wait(dve, s_scan, t + 1)
                    nc.vector.tensor_tensor(self.scan[:, 0:CH], self.scan[:, 0:CH], mask[:, ds(t * CH, CH)], ALU.mult).then_inc(s_pick, 1)
                    wait(dve, s_pick, t + 1)
                    nc.vector.tensor_tensor(self.pos_s, self.pos_s, self.scan, ALU.add).then_inc(s_pos, 1)
                    wait(dve, s_pos, t + 1)

                def back(t, p):
                    wait(dve, s_l2, t + 1)
                    wait_half(t, p)
                    nc.vector.scalar_tensor_tensor(xjo[p], bank[2 + p][:, D:2 * D], 0.0, lb[p][:, D:2 * D],
                                                   ALU.max, ALU.add).then_inc(s_xjo, 1)
                    nc.vector.scalar_tensor_tensor(V[:, ds(t * D, D)], bank[2 + p][:, 0:D], 0.0, lb[p][:, 0:D],
                                                   ALU.max, ALU.add).then_inc(s_out, 1)

                def wait_half(t, p):
                    if not isinstance(t, int):
                        wait(dve, s_wr[p], (t - p) * 8)
                    elif t >= 2:
                        wait(dve, s_wr[p], 16 * (t // 2))

                self.skewed(dve, front, back)
                nc.vector.tensor_scalar(self.scan, self.pos_s, 0.0, PADPOS, ALU.is_equal, ALU.mult).then_inc(s_fin, 1)
                wait(dve, s_fin, 1)
                nc.vector.scalar_tensor_tensor(tmp, self.pos_s, -1.0, self.scan, ALU.add, ALU.add).then_inc(s_fin, 1)
                wait(dve, s_fin, 2)


    def messages(self):
        nc, a, f32, i32 = self.nc, self.a, self.f32, self.i32
        ALU, ACT = mybir.AluOpType, mybir.ActivationFunctionType
        ds, bank, sem = bass.ds, self.bank, self.sem
        HU = U // 2
        at = [0]

        def part(n):
            at[0] += n
            return self.work[:, at[0] - n:at[0]]

        xj = [part(D) for _ in range(U)]
        msg_all = part(U * MW)
        msg3 = msg_all.rearrange("p (c w) -> p c w", w=MW)
        msg = [msg_all[:, s * MW:(s + 1) * MW] for s in range(U)]
        f = [part(HU * RBF) for _ in range(2)]
        fT = [[part(P) for _ in range(2)] for _ in range(2)]
        xidx = [part(HU).bitcast(i32) for _ in range(2)]
        pidx = [part(HU).bitcast(i32) for _ in range(2)]
        pos_s = self.pos_s.bitcast(i32)
        tmp1, tmp2 = self.scan.bitcast(i32), self.key.bitcast(i32)

        s_f = [sem(f"m_f{h}") for h in range(2)]
        s_tr, s_ft, s_mm, s_msg = sem("m_f_transposed"), sem("m_ft"), sem("m_filters"), sem("m_msg")
        s_xi, s_pi = sem("m_gather_indices"), sem("m_scatter_indices")
        s_g = [sem(f"m_gathered{s}") for s in range(U)]
        s_s = [sem(f"m_scattered{h}") for h in range(2)]
        s_key, s_cnt, s_steps, s_sums = sem("m_key"), sem("m_counted"), sem("m_base_steps"), sem("m_base_sums")
        s_eq, s_scan, s_pos, s_fin, s_init = sem("m_eq"), sem("m_scanned"), sem("m_picked"), sem("m_pos"), sem("m_init")
        s_w = sem("m_w_rel0")

        def turns(eng, body, middle=None):
            body(0)
            with eng.Fori(1, NT) as i:
                body(i)
            if middle:
                middle()
            with eng.Fori(NT, TURNS - 1) as i:
                body(i)
            body(TURNS - 1)

        assert TURNS == 2 * NT
        with nc.Block() as block:

            @block.sync
            def _(sp):
                rows = a["edge_attr_64"][0:COLS * P, :].rearrange("(p c) r -> p (c r)", c=COLS)

                def body(i):
                    for h in range(2):
                        wait(sp, s_tr, 4 * i - 2 + 2 * h)
                        if isinstance(i, int) and (U * i + HU * (h + 1)) > COLS:
                            for c in range(RESTFULL + 1):
                                n = P if c < RESTFULL else RESTPART
                                first = COLS * P + c * P
                                sp.dma_start(f[h][0:n, c * RBF:(c + 1) * RBF],
                                             a["edge_attr_64"][first:first + n, :]).then_inc(s_f[h], 16)
                        else:
                            sp.dma_start(f[h], rows[:, ds((U * i + HU * h) * RBF, HU * RBF)]).then_inc(s_f[h], 16)

                turns(sp, body)
                for k in range(2):
                    sp.dma_start(self.R0[:, k * REL * D:(k + 1) * REL * D].rearrange("p (r d) -> p r d", d=D),
                                 a["L1_gnn_W_rel"][0, :, k * P:(k + 1) * P, :].rearrange("r p d -> p r d")).then_inc(s_w, 16)
                sp.wait_ge(s_w, 32)

            @block.gpsimd
            def _(eng):
                def gathers(i, h):
                    wait(eng, s_xi, 2 * i + h + 1)
                    for j in range(HU):
                        s = HU * h + j
                        eng.indirect_dma_start(out=xj[s], out_offset=None, in_=self.xj_table,
                                               in_offset=bass.IndirectOffsetOnAxis(ap=xidx[h][:, j:j + 1], axis=0),
                                               bounds_check=N - 1, oob_is_err=False).then_inc(s_g[s], 16)

                def scatters(i, h):
                    wait(eng, s_pi, 2 * i + h + 1)
                    for j in range(HU):
                        s = HU * h + j
                        wait(eng, s_msg, U * i + s + 1)
                        eng.indirect_dma_start(out=self.msg_slots, in_=msg[s], in_offset=None,
                                               out_offset=bass.IndirectOffsetOnAxis(ap=pidx[h][:, j:j + 1], axis=0),
                                               bounds_check=NPAIR * PAIR - 1, oob_is_err=False).then_inc(s_s[h], 16)

                nc.gpsimd.memset(msg_all, 0.0).then_inc(s_init, 1)
                nc.gpsimd.memset(self.work[:, 0:U * D], 0.0).then_inc(s_init, 1)
                wait(eng, s_init, 2)
                gathers(0, 0)

                def body(i):
                    gathers(i, 1)
                    scatters(i, 0)
                    if not isinstance(i, int) or i < TURNS - 1:
                        gathers(i + 1, 0)
                    scatters(i, 1)

                turns(eng, body)
                for h in range(2):
                    wait(eng, s_s[h], 16 * HU * TURNS)

            @block.tensor
            def _(pe):
                def body(i):
                    for h in range(2):
                        last_turn = isinstance(i, int) and i == TURNS - 1
                        pe.wait_ge(s_f[h], 16 * (i + 1 + (RESTFULL if last_turn and h else 0)))
                        for pr in range(2):
                            wait(pe, s_ft, 4 * i + 2 * h + pr - 1)
                            nc.tensor.transpose(bank[4 + pr][:, h * P:(h + 1) * P],
                                                f[h][:, pr * P:(pr + 1) * P], self.ident[:, :]).then_inc(s_tr, 1)
                        for pr in range(2):
                            pe.wait_ge(s_ft, 4 * i + 2 * h + pr + 1)
                            for j in range(2):
                                wait(pe, s_msg, U * i + HU * h + 2 * pr + j - HU + 1)
                                nc.tensor.matmul(bank[2 * pr + j][:, 0:D], fT[h][pr][j * RBF:(j + 1) * RBF, :],
                                                 self.GT[j * RBF:(j + 1) * RBF, :], start=True, stop=True).then_inc(s_mm, 1)

                turns(pe, body, lambda: self.base_tensor(pe, bank[6], bank[7], (s_cnt, NT), s_steps, s_sums, False))

            @block.scalar
            def _(act):
                def body(i):
                    for h in range(2):
                        wait(act, s_mm, U * i - HU + HU * h)
                        for pr in range(2):
                            wait(act, s_tr, 4 * i + 2 * h + pr + 1)
                            nc.scalar.activation(fT[h][pr], bank[4 + pr][:, h * P:(h + 1) * P],
                                                 ACT.Copy).then_inc(s_ft, 1)

                turns(act, body)

            @block.vector
            def _(dve):
                def take(i, h):
                    nc.vector.tensor_copy(xidx[h], self.dst[:, ds(U * i + HU * h, HU)]).then_inc(s_xi, 1)

                def body(i):
                    for h in range(2):
                        wait(dve, s_s[h], 16 * HU * i)
                        nc.vector.tensor_copy(pidx[h], pos_s[:, ds(U * i + HU * h, HU)]).then_inc(s_pi, 1)
                        nc.vector.tensor_copy(msg3[:, HU * h:HU * (h + 1), D], self.loc_s[:, ds(U * i + HU * h, HU)])
                        for j in range(HU):
                            s = HU * h + j
                            wait(dve, s_mm, U * i + s + 1)
                            wait(dve, s_g[s], 16 * (i + 1))
                            nc.vector.tensor_tensor(msg[s][:, 0:D], bank[j][:, 0:D], xj[s], ALU.mult).then_inc(s_msg, 1)
                        take(i + 1, h)
                        if h == 0:
                            if isinstance(i, int) and i == 0 or not isinstance(i, int) and phase[0] == 0:
                                self.count_step(i, self.eq).then_inc(s_cnt, 1)
                                wait(dve, s_cnt, i + 1)
                            else:
                                g = i - NT
                                nc.vector.tensor_scalar(self.eq, self.key[:, 0:CH], self.iota[:, ds(g, 1)], None,
                                                        ALU.is_equal).then_inc(s_eq, 1)
                                wait(dve, s_eq, g + 1)
                                self.scan_step(g, self.eq).then_inc(s_scan, 1)
                                wait(dve, s_scan, g + 1)
                                nc.vector.copy_predicated(self.pos_d[:, 0:CH], self.eq, self.scan[:, 0:CH]).then_inc(s_pos, 1)
                                wait(dve, s_pos, g + 1)

                phase = [0]

                def middle():
                    self.base_vector(dve, bank[6], bank[7], s_steps, s_sums, self.flag_d, False)
                    phase[0] = 1

                wait(dve, s_init, 2)
                take(0, 0)
                take(0, 1)
                nc.vector.tensor_scalar(tmp1, self.dst, P.bit_length() - 1, None, ALU.logical_shift_right).then_inc(s_key, 1)
                nc.vector.memset(self.pos_d, PADPOS).then_inc(s_key, 1)
                wait(dve, s_key, 2)
                nc.vector.tensor_copy(self.key, tmp1).then_inc(s_key, 1)
                wait(dve, s_key, 3)
                turns(dve, body, middle)
                pd = self.pos_d.bitcast(i32)
                nc.vector.tensor_scalar(pd, self.pos_d, -1.0, None, ALU.add).then_inc(s_fin, 1)
                wait(dve, s_fin, 1)
                nc.vector.tensor_scalar(tmp1, pd, P - 1, None, ALU.bitwise_and).then_inc(s_fin, 1)
                nc.vector.tensor_scalar(tmp2, pd, P.bit_length() - 1, None, ALU.logical_shift_right).then_inc(s_fin, 1)
                wait(dve, s_fin, 3)
                nc.vector.scalar_tensor_tensor(pd, tmp1, float(SLOTC), tmp2, ALU.mult, ALU.add).then_inc(s_fin, 1)
                wait(dve, s_fin, 4)


    def tile_end(self, pe, flag, q, s_pair, s_tile, s_taken, seed, use=None):
        with pe.If(flag > 0):
            pe.wait_ge(s_pair, q + 1)
            pe.sem_inc(s_tile, 1)
            if use:
                with pe.If(flag > 1):
                    use(flag)
            pe.wait_ge(s_taken, flag)
            seed(flag)

    def flags(self, pe, table, q):
        return [pe.value_load(table[0:1, bass.ds(q + k, 1)], min_val=0, max_val=NT) for k in range(PB // 2)]

    def agg_pair(self, bank, chunks, hots, sem):
        for c in range(2):
            for mh in range(2):
                last = self.nc.tensor.matmul(bank[:, mh * P:(mh + 1) * P], chunks[c][:, mh * P:(mh + 1) * P], hots[c],
                                             start=False, stop=True, skip_group_check=True)
        last.then_inc(sem, 1)


    def filter_layer(self):
        nc, f32, i32 = self.nc, self.f32, self.i32
        ALU, ACT = mybir.AluOpType, mybir.ActivationFunctionType
        ds, bank, sem = bass.ds, self.bank, self.sem
        X, V, WT, R0, bias9 = self.X, self.V, self.WT, self.R0, self.bias9
        at = [0]

        def part(n):
            at[0] += n
            return self.work[:, at[0] - n:at[0]]

        lidx = [part(U // 2).bitcast(i32) for _ in range(2)]
        lrow = [part(U) for _ in range(2)]
        base_at = at[0]
        ring = [part(2 * MW) for _ in range(PB)]
        hot = [[part(P) for _ in range(2)] for _ in range(PB)]
        at[0] = base_at
        t1, H = part(1024), part(1024)
        xts = part(1024)
        xro = [part(REL * D) for _ in range(2)]
        rst = part(48)

        s_stage = sem("f_list_staged")
        s_ls = [sem(f"f_list{h}") for h in range(2)]
        s_ld = [sem(f"f_loaded{k}") for k in range(PB)]
        s_hot, s_pair, s_tile, s_taken = sem("f_hot"), sem("f_pair"), sem("f_tile"), sem("f_taken")
        s_m1, s_m2 = sem("f_m1"), sem("f_m2")
        s_abs, s_exp, s_log, s_h, s_v = sem("f_abs"), sem("f_exp"), sem("f_log"), sem("f_h"), sem("f_v")
        s_n, s_x, s_st, s_ag = sem("f_node_major"), sem("f_residual"), sem("f_stats"), sem("f_aggr")
        s_lv, s_r0, s_nw = sem("f_lnvar"), sem("f_rstd0"), sem("f_newton")
        s_h2, s_t2, s_xt, s_vt = sem("f_h2"), sem("f_h2_transposed"), sem("f_xt"), sem("f_v_written")
        s_mr, s_ea, s_ev = sem("f_rel"), sem("f_rel_act"), sem("f_rel_dve")
        s_wr = [sem(f"f_rel_written{i}") for i in range(2)]
        xr2 = self.xr[0].rearrange("(n r) d -> n (r d)", r=REL)

        NBLK = -(-NT // 4)
        tiles = lambda b: min(4, NT - 4 * b) if isinstance(b, int) else 4

        with nc.Block() as block:

            @block.gpsimd
            def _(eng):
                posd = self.pos_d.bitcast(i32)

                def body(i):
                    for h in range(2):
                        wait(eng, s_ls[h], 16 * (U // 2) * i)
                        c = U * i + U // 2 * h
                        nc.gpsimd.tensor_copy(lidx[h], posd[:, ds(c, U // 2)]).then_inc(s_stage, 1)
                        nc.gpsimd.tensor_copy(lrow[h], self.edge_row[:, ds(2 * c, U)]).then_inc(s_stage, 1)
                        wait(eng, s_stage, 4 * i + 2 * h + 2)
                        for j in range(U // 2):
                            eng.indirect_dma_start(out=self.edge_slots, in_=lrow[h][:, 2 * j:2 * j + 2], in_offset=None,
                                                   out_offset=bass.IndirectOffsetOnAxis(ap=lidx[h][:, j:j + 1], axis=0),
                                                   bounds_check=P * SLOTC - 1, oob_is_err=False).then_inc(s_ls[h], 16)

                body(0)
                with eng.Fori(1, TURNS) as i:
                    body(i)
                for h in range(2):
                    wait(eng, s_ls[h], 16 * (U // 2) * TURNS)

            @block.sync
            def _(sp):
                def load(i):
                    for k in range(PB):
                        wait(sp, s_pair, PB * i + k - PB + 1)
                        sp.dma_start(ring[k], self.msg_slots[ds((PB * i + k) * PAIR, PAIR), :].rearrange(
                            "(p j) c -> p (j c)", j=2)).then_inc(s_ld[k], 16)

                load(0)
                with sp.Fori(1, PTURNS) as i:
                    load(i)

                def write(b):
                    for j in range(tiles(b)):
                        t = 4 * b + j
                        sp.wait_ge(s_ea, 2 * (t + 1))
                        sp.wait_ge(s_ev, 2 * (t + 1))
                        sp.dma_start(xr2[ds(t * P, P), :], xro[j % 2]).then_inc(s_wr[j % 2], 16)

                with sp.Fori(0, NBLK - 1) as b:
                    write(b)
                write(NBLK - 1)
                sp.wait_ge(s_wr[0], 16 * (NT - NT // 2))
                sp.wait_ge(s_wr[1], 16 * (NT // 2))

            @block.tensor
            def _(pe):
                def seed(t):
                    nc.tensor.matmul(bank[0][:, 0:D], self.ident[:, :], V[:, ds(t * D, D)], start=True, stop=True,
                                     skip_group_check=True)

                seed(0)
                with pe.Fori(0, PTURNS) as i:
                    for k in range(PB):
                        if k % (PB // 2) == 0:
                            fl = self.flags(pe, self.flag_s, PB * i + k)
                        pe.wait_ge(s_hot, PB * i + k + 1)
                        self.agg_pair(bank[0], [ring[k][:, c * MW:c * MW + D] for c in range(2)], hot[k], s_pair)
                        self.tile_end(pe, fl[k % (PB // 2)], PB * i + k, s_pair, s_tile, s_taken, seed)
                pe.wait_ge(s_taken, NT)

                def layer(b, m, src, done):
                    n = tiles(b) * P
                    for mh in range(2):
                        o = bank[mh][:, 0:n]
                        nc.tensor.matmul(o, bias9[:, mh * P:(mh + 1) * P], self.ident[:, m:m + 1].to_broadcast([P, n]),
                                         start=True, stop=False, skip_group_check=True)
                        for k in range(2):
                            last = nc.tensor.matmul(o, WT[:, m * 512 + k * D + mh * P:m * 512 + k * D + mh * P + P], src(k),
                                                    start=False, stop=True, skip_group_check=True)
                    last.then_inc(done, 1)

                def transform(b, j):
                    t = 4 * b + j
                    pe.wait_ge(s_xt, t + 1)
                    for c in range(4):
                        if c % 2 == 0:
                            wait(pe, s_ea, 2 * t - 1 + c // 2)
                        else:
                            wait(pe, s_ev, 2 * t - 1 + c // 2)
                        for k in range(2):
                            last = nc.tensor.matmul(bank[4 + c][:, :], xts[:, j * D + k * P:j * D + (k + 1) * P],
                                                    R0[:, k * REL * D + c * 512:k * REL * D + (c + 1) * 512],
                                                    start=(k == 0), stop=(k == 1))
                        last.then_inc(s_mr, 1)

                def chain(b, before):
                    nb = tiles(b)
                    vb = V[:, ds(4 * b * D, nb * D)].rearrange("p (t k n) -> p k t n", k=2, n=P)
                    for r in range(RES):
                        wait(pe, s_v, RES * b + r)
                        if r == 0:
                            wait(pe, s_h, 4 * b)
                        layer(b, 2 + r, lambda k: vb[:, k, :, :], s_m1)
                        if before is not None and r < tiles(before):
                            transform(before, r)
                        pe.wait_ge(s_h, 4 * b + r + 1)
                        layer(b, 5 + r, lambda k: H[:, k * 512:k * 512 + nb * P], s_m2)
                    if before is not None:
                        transform(before, 3)
                    pe.wait_ge(s_h, 4 * b + 4)
                    for j in range(nb):
                        t = 4 * b + j
                        wait(pe, s_x, t - 1)
                        if j < 2:
                            wait(pe, s_xt, 4 * b)
                        o = bank[2 + j % 2][:, 0:D]
                        nc.tensor.matmul(o, self.ident[:, 8:9].to_broadcast([P, P]), bias9[:, :], start=True, stop=False,
                                         skip_group_check=True)
                        for k in range(2):
                            last = nc.tensor.matmul(o, H[:, k * 512 + j * P:k * 512 + (j + 1) * P],
                                                    WT[:, 8 * 512 + k * D:8 * 512 + (k + 1) * D], start=False, stop=True,
                                                    skip_group_check=True)
                        last.then_inc(s_n, 1)
                    for j in range(nb):
                        t = 4 * b + j
                        pe.wait_ge(s_h2, t + 1)
                        if j >= 2:
                            pe.wait_ge(s_xt, t - 1)
                        for k in range(2):
                            last = nc.tensor.transpose(bank[2 + j % 2][:, D + k * P:D + (k + 1) * P],
                                                       t1[:, j * D + k * P:j * D + (k + 1) * P], self.ident[:, :])
                        last.then_inc(s_t2, 1)

                chain(0, None)
                chain(1, 0)
                with pe.Fori(2, NBLK - 1) as b:
                    chain(b, b - 1)
                chain(NBLK - 1, NBLK - 2)
                for j in range(tiles(NBLK - 1)):
                    transform(NBLK - 1, j)

            @block.scalar
            def _(act):
                nc.scalar.preload_act_table_set("natural_log_exp_and_others")
                with act.Fori(0, NT) as t:
                    wait(act, s_tile, t + 1)
                    nc.scalar.activation(V[:, ds(t * D, D)], bank[0][:, 0:D], ACT.Copy).then_inc(s_taken, 1)
                wait(act, s_taken, NT)

                def evac(b, j):
                    t = 4 * b + j
                    if not isinstance(t, int) or t >= 2:
                        wait(act, s_wr[j % 2], 16 * (2 * b + j // 2))
                    for c in (0, 2):
                        wait(act, s_mr, 4 * t + c + 1)
                        nc.scalar.activation(xro[j % 2][:, c * 512:(c + 1) * 512], bank[4 + c][:, :], ACT.Copy).then_inc(s_ea, 1)

                def chain(b, before):
                    nb = tiles(b)
                    n = nb * P
                    for r in range(RES):
                        wait(act, s_m1, RES * b + r + 1)
                        if r == 0:
                            wait(act, s_t2, 4 * b)
                        wait(act, s_h, 4 * b + r)
                        nc.scalar.activation(t1[:, 0:n], bank[0][:, 0:n], ACT.Abs).then_inc(s_abs, 1)
                        nc.scalar.activation(t1[:, 512:512 + n], bank[1][:, 0:n], ACT.Abs).then_inc(s_abs, 1)
                        both = t1.rearrange("p (k n) -> p k n", k=2)[:, :, 0:n]
                        wait(act, s_abs, 7 * b + 2 * r + 2)
                        nc.scalar.activation(both, both, ACT.Exp, scale=-1.0).then_inc(s_exp, 1)
                        wait(act, s_exp, 4 * b + r + 1)
                        nc.scalar.activation(both, both, ACT.Ln, bias=1.0).then_inc(s_log, 1)
                        if before is not None and r < tiles(before):
                            evac(before, r)
                    wait(act, s_v, RES * b + RES)
                    wait(act, s_h, 4 * b + RES)
                    vb = V[:, ds(4 * b * D, nb * D)].rearrange("p (t k n) -> p k t n", k=2, n=P)
                    both = t1.rearrange("p (k n) -> p k n", k=2)[:, :, 0:n]
                    nc.scalar.activation(both.rearrange("p k (t n) -> p k t n", n=P), vb, ACT.Abs).then_inc(s_abs, 1)
                    wait(act, s_abs, 7 * b + 7)
                    nc.scalar.activation(both, both, ACT.Exp, scale=-1.0).then_inc(s_exp, 1)
                    wait(act, s_exp, 4 * b + 4)
                    nc.scalar.activation(both, both, ACT.Ln, bias=1.0).then_inc(s_log, 1)
                    if before is not None:
                        evac(before, 3)
                    wait(act, s_ag, 7 * b + 7)
                    nc.scalar.activation(rst[:, 0:nb], rst[:, 12:12 + nb],
                                         ACT.Ln, bias=self.epsc[:, 0:1]).then_inc(s_lv, 1)
                    wait(act, s_lv, b + 1)
                    nc.scalar.activation(rst[:, 0:nb], rst[:, 0:nb], ACT.Exp, scale=-0.5).then_inc(s_r0, 1)
                    wait(act, s_nw, 5 * b + 5)
                    wait(act, s_h, 4 * b + 4)
                    for j in range(nb):
                        nc.scalar.activation(t1[:, j * D:(j + 1) * D], X[:, ds((4 * b + j) * D, D)], ACT.Relu,
                                             bias=rst[:, 4 + j:5 + j], scale=rst[:, j:j + 1]).then_inc(s_h2, 1)
                    for j in range(nb):
                        t = 4 * b + j
                        wait(act, s_xt, t + 1)
                        nc.scalar.activation(V[:, ds(t * D, D)], xts[:, j * D:(j + 1) * D], ACT.Copy).then_inc(s_vt, 1)

                chain(0, None)
                chain(1, 0)
                with act.Fori(2, NBLK - 1) as b:
                    chain(b, b - 1)
                chain(NBLK - 1, NBLK - 2)
                for j in range(tiles(NBLK - 1)):
                    evac(NBLK - 1, j)

            @block.vector
            def _(dve):
                def hots(i):
                    for k in range(PB):
                        wait(dve, s_pair, PB * i + k - PB + 1)
                        wait(dve, s_ld[k], 16 * (i + 1))
                        nc.vector.tensor_scalar(hot[k][0], self.iota[:, :], ring[k][:, D:D + 1], None, ALU.is_equal)
                        nc.vector.tensor_scalar(hot[k][1], self.iota[:, :], ring[k][:, MW + D:MW + D + 1], None,
                                                ALU.is_equal).then_inc(s_hot, 1)

                hots(0)
                with dve.Fori(1, PTURNS) as i:
                    hots(i)
                wait(dve, s_pair, NPAIR)

                def evac(b, j):
                    t = 4 * b + j
                    if not isinstance(t, int) or t >= 2:
                        wait(dve, s_wr[j % 2], 16 * (2 * b + j // 2))
                    for c in (1, 3):
                        wait(dve, s_mr, 4 * t + c + 1)
                        nc.vector.tensor_copy(xro[j % 2][:, c * 512:(c + 1) * 512], bank[4 + c][:, :]).then_inc(s_ev, 1)

                def chain(b, before):
                    nb = tiles(b)
                    n = nb * P
                    vb = V[:, ds(4 * b * D, nb * D)].rearrange("p (t k n) -> p k t n", k=2, n=P)
                    for r in range(RES):
                        wait(dve, s_log, 4 * b + r + 1)
                        if r:
                            wait(dve, s_m2, RES * b + r)
                        else:
                            wait(dve, s_n, 4 * b)
                        for mh in range(2):
                            last = nc.vector.scalar_tensor_tensor(H[:, mh * 512:mh * 512 + n], bank[mh][:, 0:n], 0.0,
                                                                  t1[:, mh * 512:mh * 512 + n], ALU.max, ALU.add)
                        last.then_inc(s_h, 1)
                        if before is not None and r < tiles(before):
                            evac(before, r)
                        wait(dve, s_m2, RES * b + r + 1)
                        for mh in range(2):
                            last = nc.vector.tensor_tensor(vb[:, mh, :, :], vb[:, mh, :, :],
                                                           bank[mh][:, 0:n].rearrange("p (t n) -> p t n", n=P), ALU.add)
                        last.then_inc(s_v, 1)
                    wait(dve, s_v, RES * b + RES)
                    wait(dve, s_log, 4 * b + 4)
                    for mh in range(2):
                        last = nc.vector.scalar_tensor_tensor(H[:, mh * 512:mh * 512 + n].rearrange("p (t n) -> p t n", n=P),
                                                              vb[:, mh, :, :], 0.0,
                                                              t1[:, mh * 512:mh * 512 + n].rearrange("p (t n) -> p t n", n=P),
                                                              ALU.max, ALU.add)
                    last.then_inc(s_h, 1)
                    if before is not None:
                        evac(before, 3)
                    for j in range(nb):
                        t = 4 * b + j
                        wait(dve, s_n, t + 1)
                        xt = X[:, ds(t * D, D)]
                        nc.vector.tensor_tensor(xt, xt, bank[2 + j % 2][:, 0:D], ALU.add).then_inc(s_x, 1)
                        wait(dve, s_x, t + 1)
                        nc.vector.bn_stats(rst[:, 24 + 6 * j:30 + 6 * j], xt).then_inc(s_st, 1)
                    wait(dve, s_st, 4 * b + nb)
                    self.join_stats(dve, rst[:, 24:24 + 6 * nb], rst[:, 8:8 + nb], rst[:, 12:12 + nb], rst[:, 20:20 + nb],
                                    s_ag, 7 * b)
                    r_, q_, w_ = rst[:, 0:nb], rst[:, 4:4 + nb], rst[:, 16:16 + nb]
                    wait(dve, s_r0, b + 1)
                    nc.vector.tensor_tensor(w_, r_, r_, ALU.mult).then_inc(s_nw, 1)
                    wait(dve, s_nw, 5 * b + 1)
                    nc.vector.scalar_tensor_tensor(w_, rst[:, 12:12 + nb], EPS, w_, ALU.add, ALU.mult).then_inc(s_nw, 1)
                    wait(dve, s_nw, 5 * b + 2)
                    nc.vector.tensor_scalar(w_, w_, -0.5, 1.5, ALU.mult, ALU.add).then_inc(s_nw, 1)
                    wait(dve, s_nw, 5 * b + 3)
                    nc.vector.tensor_tensor(r_, r_, w_, ALU.mult).then_inc(s_nw, 1)
                    wait(dve, s_nw, 5 * b + 4)
                    nc.vector.scalar_tensor_tensor(q_, rst[:, 8:8 + nb], -1.0, r_, ALU.mult, ALU.mult).then_inc(s_nw, 1)
                    if before is not None:
                        wait(dve, s_mr, 16 * before + 16)
                        wait(dve, s_vt, 4 * b)
                    for j in range(nb):
                        t = 4 * b + j
                        wait(dve, s_t2, t + 1)
                        nc.vector.tensor_copy(xts[:, j * D:(j + 1) * D], bank[2 + j % 2][:, D:2 * D]).then_inc(s_xt, 1)

                wait(dve, s_taken, NT)
                chain(0, None)
                chain(1, 0)
                with dve.Fori(2, NBLK - 1) as b:
                    chain(b, b - 1)
                chain(NBLK - 1, NBLK - 2)
                for j in range(tiles(NBLK - 1)):
                    evac(NBLK - 1, j)


    def relational_layer(self, l):
        nc, a, f32, i32 = self.nc, self.a, self.f32, self.i32
        ALU, ACT = mybir.AluOpType, mybir.ActivationFunctionType
        ds, bank, sem = bass.ds, self.bank, self.sem
        X, V = self.X, self.V
        last_layer = l == LAYERS - 1
        at = [0]

        def part(n):
            at[0] += n
            return self.work[:, at[0] - n:at[0]]

        ring = [[part(D) for _ in range(2)] for _ in range(PB)]
        hot = [[part(P) for _ in range(2)] for _ in range(PB // 2)]
        gidx = [part(4).bitcast(i32) for _ in range(PB // 2)]
        xts = part(D)
        xro = [part(REL * D) for _ in range(2)]
        listed = self.idx[:, 0:2 * SLOTC]
        rows = self.idx[:, 2 * SLOTC:3 * SLOTC].bitcast(i32)
        node = self.idx[:, 3 * SLOTC:4 * SLOTC]
        roots = [self.idx[:, 5 * IW + 512 * k:5 * IW + 512 * (k + 1)] for k in range(LAYERS)]
        rel = self.WT[:, 0:2 * REL * D] if l == 0 else self.R0[:, :]
        table = self.xr[l % 2]
        nxt = self.xr[(l + 1) % 2].rearrange("(n r) d -> n (r d)", r=REL)
        nm = f"r{l}_"
        if l == 0:
            s_li, s_ii = sem(nm + "list_loaded"), sem(nm + "list_split")
        s_init, s_gi = sem(nm + "ring_zeroed"), sem(nm + "gather_indices")
        s_in = self.s_in

        def arrived(turns):
            return 32 * (turns + PTURNS * l)

        s_hot, s_pair, s_tile, s_taken = sem(nm + "hot"), sem(nm + "pair"), sem(nm + "tile"), sem(nm + "taken")
        s_xt, s_mr = sem(nm + "xt"), sem(nm + "rel")
        if last_layer:
            s_kept, s_res, s_out = sem(nm + "kept"), sem(nm + "residual"), sem(nm + "out")
        else:
            s_w, s_ea = sem(nm + "weights"), sem(nm + "rel_out")
            s_wr = [sem(f"{nm}written{i}") for i in range(2)]

        with nc.Block() as block:

            @block.sync
            def _(sp):
                if l == 0:
                    sp.dma_start(listed, self.edge_slots.rearrange("(p c) two -> p (c two)", p=P)).then_inc(s_li, 16)
                    for k in range(LAYERS):
                        sp.dma_start(roots[k].rearrange("p (h d) -> p h d", h=2),
                                     a["L1_gnn_W_root"][k, :, :].rearrange("(h p) d -> p h d", p=P)).then_inc(s_w, 16)
                if not last_layer:
                    for k in range(2):
                        sp.dma_start(rel[:, k * REL * D:(k + 1) * REL * D].rearrange("p (r d) -> p r d", d=D),
                                     a["L1_gnn_W_rel"][l + 1, :, k * P:(k + 1) * P, :].rearrange("r p d -> p r d")).then_inc(s_w, 16)

                    def write(t, p):
                        sp.wait_ge(s_ea, 4 * t + 15)
                        sp.dma_start(nxt[ds(t * P, P), :], xro[p]).then_inc(s_wr[p], 16)

                    with sp.Fori(0, NT // 2) as i:
                        write(2 * i, 0)
                        write(2 * i + 1, 1)
                    write(NT - 1, 0)
                    sp.wait_ge(s_wr[0], 16 * (NT - NT // 2))
                    sp.wait_ge(s_wr[1], 16 * (NT // 2))
                else:
                    G = 7
                    with sp.Fori(0, NT // G - 1) as i:
                        sp.wait_ge(s_res, i + 1)
                        sp.dma_start(a["out"][ds(i * G * P, G * P), :].rearrange("(t p) d -> p t d", p=P),
                                     X[:, ds(i * G * D, G * D)].rearrange("p (t d) -> p t d", d=D)).then_inc(s_out, 16)
                    sp.wait_ge(s_res, NT // G)
                    sp.dma_start(a["out"][(NT - G) * P:(NT - 1) * P, :].rearrange("(t p) d -> p t d", p=P),
                                 X[:, (NT - G) * D:(NT - 1) * D].rearrange("p (t d) -> p t d", d=D)).then_inc(s_out, 16)
                    sp.dma_start(a["out"][(NT - 1) * P:N, :], X[0:TAILROWS, (NT - 1) * D:NT * D]).then_inc(s_out, 16)
                    sp.wait_ge(s_out, 16 * (NT // G + 1))
                if l == 0:
                    sp.wait_ge(s_w, 16 * (LAYERS + 2))
                elif not last_layer:
                    sp.wait_ge(s_w, 32)

            @block.gpsimd
            def _(eng):
                nc.gpsimd.memset(self.work[:, 0:2 * PB * D], 0.0).then_inc(s_init, 1)
                wait(eng, s_init, 1)

                def body(i):
                    for q in range(PB // 2):
                        wait(eng, s_gi, PB // 2 * i + q + 1)
                        for k in range(2):
                            pair = 2 * q + k
                            wait(eng, s_pair, PB * (i - 1) + pair + 1)
                            for c in range(2):
                                j = 2 * k + c
                                eng.indirect_dma_start(out=ring[pair][c], out_offset=None, in_=table,
                                                       in_offset=bass.IndirectOffsetOnAxis(ap=gidx[q][:, j:j + 1], axis=0),
                                                       bounds_check=N * REL - 1, oob_is_err=False).then_inc(s_in[pair], 16)

                body(0)
                with eng.Fori(1, PTURNS) as i:
                    body(i)

            @block.vector
            def _(dve):
                if l == 0:
                    wait(dve, s_li, 16)
                    l2 = listed.rearrange("p (c two) -> p c two", two=2)
                    nc.vector.tensor_copy(rows, l2[:, :, 0]).then_inc(s_ii, 1)
                    nc.vector.tensor_copy(node, l2[:, :, 1]).then_inc(s_ii, 1)
                    wait(dve, s_ii, 2)

                def take(i, q):
                    for k in range(2):
                        wait(dve, s_in[2 * q + k], arrived(i))
                    nc.vector.tensor_copy(gidx[q], rows[:, ds(2 * PB * i + 4 * q, 4)]).then_inc(s_gi, 1)

                def body(i):
                    for q in range(PB // 2):
                        if q < 2:
                            take(i, q + 2)
                        elif not (isinstance(i, int) and i == PTURNS - 1):
                            take(i + 1, q - 2)
                        for k in range(2):
                            pair = 2 * q + k
                            wait(dve, s_pair, PB * i + pair - PB // 2 + 1)
                            for c in range(2):
                                last = nc.vector.tensor_scalar(hot[pair % (PB // 2)][c], self.iota[:, :],
                                                               node[:, ds(2 * (PB * i + pair) + c, 1)], None, ALU.is_equal)
                            last.then_inc(s_hot, 1)

                take(0, 0)
                take(0, 1)
                body(0)
                with dve.Fori(1, PTURNS - 1) as i:
                    body(i)
                body(PTURNS - 1)
                if last_layer:
                    G = 7
                    wait(dve, s_kept, NT + 2)
                    with dve.Fori(0, NT // G) as i:
                        xg = X[:, ds(i * G * D, G * D)]
                        nc.vector.tensor_tensor(xg, xg, V[:, ds(i * G * D, G * D)], ALU.add).then_inc(s_res, 1)

            @block.scalar
            def _(act):
                def take(t):
                    wait(act, s_tile, t + 1)
                    for mh in range(2):
                        last = nc.scalar.activation(V[:, ds(t * D + mh * P, P)], bank[0][:, mh * P:(mh + 1) * P], ACT.Relu,
                                                    bias=self.bcol[:, 2 * l + mh:2 * l + mh + 1])
                    last.then_inc(s_taken, 1)

                def out(t, p):
                    if last_layer:
                        wait(act, s_mr, t + 1)
                        wait(act, s_xt, t + 2)
                        nc.scalar.activation(V[:, ds(t * D, D)], bank[1][:, 0:D], ACT.Copy).then_inc(s_kept, 1)
                        return
                    for c in range(4):
                        wait(act, s_mr, 4 * t + c + 1)
                        if c == 0:
                            if not isinstance(t, int):
                                wait(act, s_wr[p], 8 * (t - p))
                            elif t >= 2:
                                wait(act, s_wr[p], 16 * (t // 2))
                        nc.scalar.activation(xro[p][:, c * 512:(c + 1) * 512], bank[4 + c][:, :], ACT.Copy).then_inc(s_ea, 1)

                def hand(t):
                    wait(act, s_taken, t + 1)
                    nc.scalar.activation(xts, V[:, ds(t * D, D)], ACT.Copy).then_inc(s_xt, 1)

                def tile(t, p):
                    take(t)
                    out(t - 1, 1 - p)
                    hand(t)

                act.sem_inc(s_xt, 1)
                act.sem_inc(s_kept if last_layer else s_ea, 2 if last_layer else 11)
                take(0)
                hand(0)
                tile(1, 1)
                tile(2, 0)
                tile(3, 1)
                with act.Fori(2, NT // 2) as i:
                    tile(2 * i, 0)
                    tile(2 * i + 1, 1)
                tile(NT - 1, 0)
                out(NT - 1, 0)

            @block.tensor
            def _(pe):
                def seed(t):
                    for mh in range(2):
                        for k in range(2):
                            nc.tensor.matmul(bank[0][:, mh * P:(mh + 1) * P], roots[l][:, k * D + mh * P:k * D + mh * P + P],
                                             V[:, ds(t * D + k * P, P)], start=(mh == 0 and k == 0), stop=True,
                                             skip_group_check=True)

                def use(t2):
                    pe.wait_ge(s_xt, t2)
                    if last_layer:
                        pe.wait_ge(s_kept, t2)
                        for k in range(2):
                            last = nc.tensor.transpose(bank[1][:, k * P:(k + 1) * P], xts[:, k * P:(k + 1) * P], self.ident[:, :])
                        last.then_inc(s_mr, 1)
                        return
                    for c in range(4):
                        pe.wait_ge(s_ea, 4 * t2 + c)
                        for k in range(2):
                            last = nc.tensor.matmul(bank[4 + c][:, :], xts[:, k * P:(k + 1) * P],
                                                    rel[:, k * REL * D + c * 512:k * REL * D + (c + 1) * 512],
                                                    start=(k == 0), stop=(k == 1))
                        last.then_inc(s_mr, 1)

                if l == 0:
                    pe.wait_ge(s_w, 16 * (LAYERS + 2))
                elif not last_layer:
                    pe.wait_ge(s_w, 32)
                seed(0)
                with pe.Fori(0, PTURNS) as i:
                    for k in range(PB):
                        if k % (PB // 2) == 0:
                            fl = self.flags(pe, self.flag_d, PB * i + k)
                        pe.wait_ge(s_hot, PB * i + k + 1)
                        pe.wait_ge(s_in[k], arrived(i + 1))
                        self.agg_pair(bank[0], ring[k], hot[k % (PB // 2)], s_pair)
                        self.tile_end(pe, fl[k % (PB // 2)], PB * i + k, s_pair, s_tile, s_taken, seed, use)
                use(NT + 1)


    def skewed(self, eng, front, back):
        front(0, 0)
        front(1, 1)
        back(0, 0)
        front(2, 0)
        back(1, 1)
        with eng.Fori(1, NT // 2) as i:
            front(2 * i + 1, 1)
            back(2 * i, 0)
            front(2 * i + 2, 0)
            back(2 * i + 1, 1)
        back(NT - 1, 0)


def build(nc, a):
    with ExitStack() as ctx:
        p = Program(nc, ctx, a)
        p.prepare()
        p.messages()
        p.filter_layer()
        for l in range(LAYERS):
            p.relational_layer(l)


_INS = ["x", "src", "dst", "edge_attr_64", "edge_type_8", "L0_gnn_G", "L0_gnn_Wi", "L0_gnn_bi", "L0_gnn_Wj",
        "L0_gnn_bj", "L0_gnn_res_w1", "L0_gnn_res_b1", "L0_gnn_res_w2", "L0_gnn_res_b2", "L0_gnn_Wv", "L0_gnn_bv",
        "L1_gnn_W_rel", "L1_gnn_W_root", "L1_gnn_bias"]


def kernel(**inputs):
    import numpy as _np
    import concourse.bacc as _bacc
    from concourse import mybir as _mybir
    from concourse.bass_utils import run_bass_kernel_spmd as _run

    nc = _bacc.Bacc("TRN2", target_bir_lowering=False, num_devices=1)
    arrays, args = {}, {}
    for name in _INS:
        x = _np.ascontiguousarray(inputs[name])
        arrays[f"in_{name}_dram"] = x
        args[name] = nc.dram_tensor(f"in_{name}_dram", x.shape, _mybir.dt.from_np(x.dtype), kind="ExternalInput").ap()
    args["out"] = nc.dram_tensor("out_0_dram", (N, D), _mybir.dt.float32, kind="ExternalOutput").ap()
    build(nc, args)
    r = _run(nc, [arrays], core_ids=[0])
    return r.results[0]["out_0_dram"]
```
